# Optimizing a Trainium2 kernel written in Bass

```python
import numpy as np
import jax
import jax.numpy as jnp

def _softmax(x, axis=-1):
    return jax.nn.softmax(x, axis=axis)

def _gelu(x):
    return jax.nn.gelu(x, approximate=True)

def _silu(x):
    return jax.nn.silu(x)

def _sigmoid(x):
    return jax.nn.sigmoid(x)

def _layernorm(x, axis=-1, eps=1e-05):
    m = jnp.mean(x, axis=axis, keepdims=True)
    v = jnp.var(x, axis=axis, keepdims=True)
    return (x - m) / jnp.sqrt(v + eps)

def _scatter_add(tgt, idx, src, axis=0):
    return tgt.at[idx].add(src)

def _segment_sum(src, seg, n):
    return jax.ops.segment_sum(src, seg, n)
kernel_name = 'mk_dlrm_tower_d1_rec_r8_a422c8'

def setup_inputs(seed: int=0):
    np.random.seed(seed)
    _w = jnp.asarray

    def _rec_inputs():
        import jax
        import jax.numpy as jnp
        _tk = jax.random.key(seed)
        ids = jnp.stack([jax.random.randint(jax.random.fold_in(_tk, 200 + f), (512,), 0, v, jnp.int32) for f, v in enumerate([125000, 12500, 12500, 1250, 1250, 1000, 1000, 12500, 12500, 12500, 12500, 1000, 1000, 12500, 1250, 1250, 1000, 1000, 1000, 1000, 1250, 12500, 1250, 1250, 1250, 1250])], axis=1)
        tbl_0 = 0.05 * jax.random.normal(jax.random.fold_in(_tk, 500 + 0), (125000, 128), jnp.float32)
        tbl_1 = 0.05 * jax.random.normal(jax.random.fold_in(_tk, 500 + 1), (12500, 128), jnp.float32)
        tbl_2 = 0.05 * jax.random.normal(jax.random.fold_in(_tk, 500 + 2), (12500, 128), jnp.float32)
        tbl_3 = 0.05 * jax.random.normal(jax.random.fold_in(_tk, 500 + 3), (1250, 128), jnp.float32)
        tbl_4 = 0.05 * jax.random.normal(jax.random.fold_in(_tk, 500 + 4), (1250, 128), jnp.float32)
        tbl_5 = 0.05 * jax.random.normal(jax.random.fold_in(_tk, 500 + 5), (1000, 128), jnp.float32)
        tbl_6 = 0.05 * jax.random.normal(jax.random.fold_in(_tk, 500 + 6), (1000, 128), jnp.float32)
        tbl_7 = 0.05 * jax.random.normal(jax.random.fold_in(_tk, 500 + 7), (12500, 128), jnp.float32)
        tbl_8 = 0.05 * jax.random.normal(jax.random.fold_in(_tk, 500 + 8), (12500, 128), jnp.float32)
        tbl_9 = 0.05 * jax.random.normal(jax.random.fold_in(_tk, 500 + 9), (12500, 128), jnp.float32)
        tbl_10 = 0.05 * jax.random.normal(jax.random.fold_in(_tk, 500 + 10), (12500, 128), jnp.float32)
        tbl_11 = 0.05 * jax.random.normal(jax.random.fold_in(_tk, 500 + 11), (1000, 128), jnp.float32)
        tbl_12 = 0.05 * jax.random.normal(jax.random.fold_in(_tk, 500 + 12), (1000, 128), jnp.float32)
        tbl_13 = 0.05 * jax.random.normal(jax.random.fold_in(_tk, 500 + 13), (12500, 128), jnp.float32)
        tbl_14 = 0.05 * jax.random.normal(jax.random.fold_in(_tk, 500 + 14), (1250, 128), jnp.float32)
        tbl_15 = 0.05 * jax.random.normal(jax.random.fold_in(_tk, 500 + 15), (1250, 128), jnp.float32)
        tbl_16 = 0.05 * jax.random.normal(jax.random.fold_in(_tk, 500 + 16), (1000, 128), jnp.float32)
        tbl_17 = 0.05 * jax.random.normal(jax.random.fold_in(_tk, 500 + 17), (1000, 128), jnp.float32)
        tbl_18 = 0.05 * jax.random.normal(jax.random.fold_in(_tk, 500 + 18), (1000, 128), jnp.float32)
        tbl_19 = 0.05 * jax.random.normal(jax.random.fold_in(_tk, 500 + 19), (1000, 128), jnp.float32)
        tbl_20 = 0.05 * jax.random.normal(jax.random.fold_in(_tk, 500 + 20), (1250, 128), jnp.float32)
        tbl_21 = 0.05 * jax.random.normal(jax.random.fold_in(_tk, 500 + 21), (12500, 128), jnp.float32)
        tbl_22 = 0.05 * jax.random.normal(jax.random.fold_in(_tk, 500 + 22), (1250, 128), jnp.float32)
        tbl_23 = 0.05 * jax.random.normal(jax.random.fold_in(_tk, 500 + 23), (1250, 128), jnp.float32)
        tbl_24 = 0.05 * jax.random.normal(jax.random.fold_in(_tk, 500 + 24), (1250, 128), jnp.float32)
        tbl_25 = 0.05 * jax.random.normal(jax.random.fold_in(_tk, 500 + 25), (1250, 128), jnp.float32)
        _rk = jax.random.fold_in(_tk, 7)
        r_dense_x = -0.000514642 + 1.00011 * jax.random.normal(jax.random.fold_in(_rk, 101), (512, 128), jnp.float32)
        W_top1 = 0.0456912 * jax.random.normal(jax.random.fold_in(_tk, 801), (479, 512), jnp.float32)
        W_top2 = 0.0441942 * jax.random.normal(jax.random.fold_in(_tk, 802), (512, 256), jnp.float32)
        W_top3 = 0.0625 * jax.random.normal(jax.random.fold_in(_tk, 803), (256, 1), jnp.float32)
        b_top1 = jnp.zeros((512,), jnp.float32)
        b_top2 = jnp.zeros((256,), jnp.float32)
        return (r_dense_x, ids, tbl_0, tbl_1, tbl_2, tbl_3, tbl_4, tbl_5, tbl_6, tbl_7, tbl_8, tbl_9, tbl_10, tbl_11, tbl_12, tbl_13, tbl_14, tbl_15, tbl_16, tbl_17, tbl_18, tbl_19, tbl_20, tbl_21, tbl_22, tbl_23, tbl_24, tbl_25, W_top1, b_top1, W_top2, b_top2, W_top3)
    r_dense_x, ids, tbl_0, tbl_1, tbl_2, tbl_3, tbl_4, tbl_5, tbl_6, tbl_7, tbl_8, tbl_9, tbl_10, tbl_11, tbl_12, tbl_13, tbl_14, tbl_15, tbl_16, tbl_17, tbl_18, tbl_19, tbl_20, tbl_21, tbl_22, tbl_23, tbl_24, tbl_25, W_top1, b_top1, W_top2, b_top2, W_top3 = _rec_inputs()

    def _L0_rec_setup():
        import jax, jax.numpy as jnp
        import numpy as np
        F = 26
        D = 128
        B = 2048
        _TRIU_I, _TRIU_J = np.triu_indices(F + 1, k=1)
        _TRIU_I = jnp.asarray(_TRIU_I)
        _TRIU_J = jnp.asarray(_TRIU_J)
        key = jax.random.key(seed)
        k1, k2 = jax.random.split(key)
        sparse_x = jax.random.normal(k1, (B, F, D), dtype=jnp.float32)
        dense_x = jax.random.normal(k2, (B, D), dtype=jnp.float32)
        return {'sparse_x': sparse_x, 'dense_x': dense_x}
    _L0_rec_all = _L0_rec_setup()
    _L0_rec_in = {k: v for k, v in _L0_rec_all.items() if k in ()}
    del _L0_rec_all
    return {'r_dense_x': r_dense_x, 'ids': ids, 'tbl_0': tbl_0, 'tbl_1': tbl_1, 'tbl_2': tbl_2, 'tbl_3': tbl_3, 'tbl_4': tbl_4, 'tbl_5': tbl_5, 'tbl_6': tbl_6, 'tbl_7': tbl_7, 'tbl_8': tbl_8, 'tbl_9': tbl_9, 'tbl_10': tbl_10, 'tbl_11': tbl_11, 'tbl_12': tbl_12, 'tbl_13': tbl_13, 'tbl_14': tbl_14, 'tbl_15': tbl_15, 'tbl_16': tbl_16, 'tbl_17': tbl_17, 'tbl_18': tbl_18, 'tbl_19': tbl_19, 'tbl_20': tbl_20, 'tbl_21': tbl_21, 'tbl_22': tbl_22, 'tbl_23': tbl_23, 'tbl_24': tbl_24, 'tbl_25': tbl_25, 'W_top1': W_top1, 'b_top1': b_top1, 'W_top2': W_top2, 'b_top2': b_top2, 'W_top3': W_top3}

def reference(r_dense_x, ids, tbl_0, tbl_1, tbl_2, tbl_3, tbl_4, tbl_5, tbl_6, tbl_7, tbl_8, tbl_9, tbl_10, tbl_11, tbl_12, tbl_13, tbl_14, tbl_15, tbl_16, tbl_17, tbl_18, tbl_19, tbl_20, tbl_21, tbl_22, tbl_23, tbl_24, tbl_25, W_top1, b_top1, W_top2, b_top2, W_top3):
    import jax
    import jax.numpy as jnp

    def _L0_rec_ref(sparse_x, dense_x):
        import jax, jax.numpy as jnp
        import numpy as np
        F = 26
        D = 128
        B = 2048
        _TRIU_I, _TRIU_J = np.triu_indices(F + 1, k=1)
        _TRIU_I = jnp.asarray(_TRIU_I)
        _TRIU_J = jnp.asarray(_TRIU_J)
        combined = jnp.concatenate([sparse_x, dense_x[:, None, :]], axis=1)
        interact = jnp.einsum('bfd,bgd->bfg', combined, combined)
        return interact[:, _TRIU_I, _TRIU_J]
    e = jnp.stack([tbl_0[ids[:, 0]], tbl_1[ids[:, 1]], tbl_2[ids[:, 2]], tbl_3[ids[:, 3]], tbl_4[ids[:, 4]], tbl_5[ids[:, 5]], tbl_6[ids[:, 6]], tbl_7[ids[:, 7]], tbl_8[ids[:, 8]], tbl_9[ids[:, 9]], tbl_10[ids[:, 10]], tbl_11[ids[:, 11]], tbl_12[ids[:, 12]], tbl_13[ids[:, 13]], tbl_14[ids[:, 14]], tbl_15[ids[:, 15]], tbl_16[ids[:, 16]], tbl_17[ids[:, 17]], tbl_18[ids[:, 18]], tbl_19[ids[:, 19]], tbl_20[ids[:, 20]], tbl_21[ids[:, 21]], tbl_22[ids[:, 22]], tbl_23[ids[:, 23]], tbl_24[ids[:, 24]], tbl_25[ids[:, 25]]], axis=1)
    z = _L0_rec_ref(e, r_dense_x)
    z = z.reshape(z.shape[0], -1)
    h = jnp.concatenate([z, r_dense_x], axis=1)
    h = jnp.maximum(h @ W_top1 + b_top1, 0.0)
    h = jnp.maximum(h @ W_top2 + b_top2, 0.0)
    y = h @ W_top3
    return y

_drawn_inputs = setup_inputs


def setup_inputs(seed=0):
    import zlib

    import numpy as np

    out = dict(_drawn_inputs(seed))
    spreads = {'b_top1': (0.0, 0.1), 'b_top2': (0.0, 0.1)}
    factors = {}
    for name, (base, spread) in spreads.items():
        noise = np.random.default_rng([zlib.crc32(name.encode()), seed]).standard_normal(out[name].shape)
        drawn = base * np.exp(spread * noise) if base else spread * noise
        out[name] = jnp.asarray(drawn.astype(out[name].dtype))
    for name, factor in factors.items():
        out[name] = (out[name] * factor).astype(out[name].dtype)
    return out
```

```python
import numpy as np
import concourse.bass as bass
from concourse import mybir
from contextlib import ExitStack

B = 512
D = 128
F = 26
NF = F + 1
H1, H2 = 512, 256
P = 128
QP = 32
QUADS = P // QP

TILE_B = 128
TURNS = B // TILE_B
UNIT_B = 64
UNITS = TILE_B // UNIT_B
FPG = P // UNIT_B
GATHERS = F // FPG
SLOTS = UNITS * GATHERS
GPT = 4
TPT = -(-GATHERS // GPT)
ET_BANKS = 4
CLASS_B = UNIT_B // QUADS
GW = 28
JB = GW // QUADS
N1 = H1 // P
N2 = H2 // P


def interaction_kernel(nc, xt_rows, ids, base, table, w1z, w1x, b1, w2, b2, w3, out):
    fp32 = mybir.dt.float32
    i32 = mybir.dt.int32
    ALU = mybir.AluOpType
    ACT = mybir.ActivationFunctionType

    ctx = ExitStack()
    with ctx:
        def sb(name, shape, dt=fp32):
            return ctx.enter_context(nc.sbuf_tensor(name, shape, dt))

        def pb(name, shape):
            return ctx.enter_context(nc.psum_tensor(name, shape, fp32))

        def sem(name):
            return ctx.enter_context(nc.semaphore(name))

        ids_sb = sb("ids_sb", [P, TURNS * SLOTS], i32)
        idx_all = sb("idx_all", [P, (TURNS + 1) * SLOTS], i32)
        base_sb = sb("base_sb", [P, GATHERS], i32)
        idx_now = sb("idx_now", [P, UNITS, GATHERS], i32)
        rows = sb("rows", [P, SLOTS, D])
        x_rows = sb("x_rows", [UNIT_B, B // UNIT_B, D])
        x_now = sb("x_now", [UNIT_B, UNITS, D])
        ident = sb("ident", [P, P])
        ct = sb("ct", [P, UNITS, UNIT_B, QP])
        xt = sb("xt", [P, TILE_B])
        z = sb("z", [P, JB, TILE_B])
        w1z_sb = sb("w1z_sb", [P, JB, H1])
        w1x_sb = sb("w1x_sb", [D, H1])
        w2_sb = sb("w2_sb", [P, N1, H2])
        w3_sb = sb("w3_sb", [P, N2])
        b1_sb = sb("b1_sb", [P, N1])
        b2_sb = sb("b2_sb", [P, N2])
        h1 = sb("h1", [P, N1, TILE_B])
        h2 = sb("h2", [P, N2, TILE_B])
        y_sb = sb("y_sb", [1, B])

        p_et = [pb(f"p_et{k}", [P, 512]) for k in range(ET_BANKS)]
        p_gram = [pb(f"p_gram{u}", [P, CLASS_B, GW]) for u in range(UNITS)]
        p_mlp = [pb(f"p_mlp{k}", [P, 4, TILE_B]) for k in range(2)]
        p_h1 = [p_mlp[n * 2 // N1][:, n % (N1 // 2), :] for n in range(N1)]
        p_h2 = [p_mlp[n][:, N1 // 2, :] for n in range(N2)]
        p_y = p_mlp[1][0:1, 3, :]

        s_ids = sem("s_ids")
        s_x = sem("s_x")
        s_w = sem("s_w")
        s_idx_all = sem("s_idx_all")
        s_ct_zero = sem("s_ct_zero")
        s_idx = [sem(f"s_idx{u}") for u in range(UNITS)]
        s_row = [sem(f"s_row{g}") for g in range(SLOTS)]
        s_xnow = sem("s_xnow")
        s_et = [sem(f"s_et{t}") for t in range(UNITS * TPT)]
        s_ct = [sem(f"s_ct{t}") for t in range(UNITS * TPT)]
        s_xt = [sem(f"s_xt{u}") for u in range(UNITS)]
        s_gram = [sem(f"s_gram{u}") for u in range(UNITS)]
        s_z_dve = [sem(f"s_z_dve{u}") for u in range(UNITS)]
        s_z_act = [sem(f"s_z_act{u}") for u in range(UNITS)]
        s_h1p = sem("s_h1p")
        s_h1_dve = sem("s_h1_dve")
        s_h1_act = sem("s_h1_act")
        s_h2p = sem("s_h2p")
        s_h2_dve = sem("s_h2_dve")
        s_h2_act = sem("s_h2_act")
        s_yp = sem("s_yp")
        s_y = sem("s_y")
        s_out = sem("s_out")
        s_ident = sem("s_ident")
        s_units = sem("s_units")

        block = ctx.enter_context(nc.Block())

        def gathers_of(t):
            return range(t * GPT, min((t + 1) * GPT, GATHERS))

        def copy_tile(engine, copy, i, u, t):
            n = UNIT_B * (FPG * len(gathers_of(t)) + (t == TPT - 1))
            tile = u * TPT + t
            engine.wait_ge(s_et[tile], i + 1)
            if t == 0:
                engine.wait_ge(s_gram[u], i)
            f0 = t * GPT * FPG
            src = p_et[tile % ET_BANKS][:, 0:n].rearrange("p (f s) -> p s f", s=UNIT_B)
            copy(ct[:, u, :, f0:f0 + n // UNIT_B], src).then_inc(s_ct[tile], 1)

        def copy_z(engine, copy, i, u, classes, done):
            engine.wait_ge(s_gram[u], i + 1)
            engine.wait_ge(s_h1p, i)
            for s in classes:
                for j in range(QUADS):
                    b0 = u * UNIT_B + s * CLASS_B
                    last = copy(z[QP * j:QP * (j + 1), :, b0:b0 + CLASS_B],
                                p_gram[u][QP * s:QP * (s + 1), :, JB * j:JB * (j + 1)].rearrange("p b g -> p g b"))
            last.then_inc(done[u], 1)

        @block.sync
        def _(sp):
            sp.dma_start(ids_sb[:], ids).then_inc(s_ids, 16)
            sp.dma_start(base_sb[:], base).then_inc(s_ids, 16)
            sp.dma_start(x_rows[:], xt_rows).then_inc(s_x, 16)
            sp.dma_start(w1x_sb[:], w1x).then_inc(s_w, 16)
            sp.dma_start(w1z_sb[:], w1z).then_inc(s_w, 16)
            sp.dma_start(w2_sb[:], w2).then_inc(s_w, 16)
            sp.dma_start(w3_sb[:], w3).then_inc(s_w, 16)
            sp.dma_start(b1_sb[:], b1).then_inc(s_w, 16)
            sp.dma_start(b2_sb[:], b2).then_inc(s_w, 16)
            sp.wait_ge(s_y, TURNS)
            sp.dma_start(out, y_sb[:]).then_inc(s_out, 16)
            sp.wait_ge(s_out, 16)

        @block.gpsimd
        def _(pool):
            nc.gpsimd.memset(ident[:], 0.0).then_inc(s_ident, 1)
            pool.wait_ge(s_ident, 1)
            nc.gpsimd.affine_select(out=ident[:], in_=ident[:], compare_op=ALU.not_equal, fill=1.0, base=0,
                                    pattern=[[-1, P]], channel_multiplier=1).then_inc(s_ident, 1)
            with pool.Fori(0, TURNS) as i:
                for u in range(UNITS):
                    pool.wait_ge(s_idx[u], i + 1)
                    pool.sem_inc(s_units, 1)
                    for t in range(TPT):
                        for g in gathers_of(t):
                            slot = u * GATHERS + g
                            pool.indirect_dma_start(
                                out=rows[:, slot, :], out_offset=None, in_=table,
                                in_offset=bass.IndirectOffsetOnAxis(ap=idx_now[:, u, g:g + 1], axis=0),
                            ).then_inc(s_row[slot], 16)

        @block.vector
        def _(dve):
            nc.vector.memset(idx_all[:, TURNS * SLOTS:], 0).then_inc(s_idx_all, 1)
            dve.wait_ge(s_ids, 32)
            nc.vector.tensor_tensor(
                idx_all[:, 0:TURNS * SLOTS].rearrange("p (v g) -> p v g", g=GATHERS),
                ids_sb[:].rearrange("p (v g) -> p v g", g=GATHERS),
                base_sb[:].rearrange("p (a g) -> p a g", a=1).broadcast_to([P, TURNS * UNITS, GATHERS]),
                ALU.add).then_inc(s_idx_all, 1)
            dve.wait_ge(s_idx_all, 2)
            for u in range(UNITS):
                nc.vector.tensor_copy(idx_now[:, u, :], idx_all[:, u * GATHERS:(u + 1) * GATHERS]).then_inc(s_idx[u], 1)
            nc.vector.memset(ct[:], 0.0).then_inc(s_ct_zero, 1)
            dve.wait_ge(s_ct_zero, 1)
            with dve.Fori(0, TURNS) as i:
                for u in range(UNITS):
                    for t in range(0, TPT, 2):
                        copy_tile(dve, nc.vector.tensor_copy, i, u, t)
                    for t in range(TPT):
                        dve.wait_ge(s_et[u * TPT + t], i + 1)
                    nc.vector.tensor_copy(idx_now[:, u, :], idx_all[:, bass.ds((i + 1) * SLOTS + u * GATHERS, GATHERS)])\
                        .then_inc(s_idx[u], 1)
                    copy_z(dve, nc.vector.tensor_copy, i, u, range(0, QUADS, 2), s_z_dve)
                dve.wait_ge(s_h1p, i + 1)
                for n in range(0, N1 // 2):
                    last = nc.vector.tensor_scalar(h1[:, n, :], p_h1[n], b1_sb[:, n:n + 1], 0.0, ALU.add, ALU.max)
                last.then_inc(s_h1_dve, 1)
                dve.wait_ge(s_h2p, i + 1)
                nc.vector.tensor_scalar(h2[:, 0, :], p_h2[0], b2_sb[:, 0:1], 0.0, ALU.add,
                                        ALU.max).then_inc(s_h2_dve, 1)
                dve.wait_ge(s_yp, i + 1)
                nc.vector.tensor_copy(y_sb[0:1, bass.ds(i * TILE_B, TILE_B)], p_y).then_inc(s_y, 1)

        @block.scalar
        def _(act):
            act.wait_ge(s_ct_zero, 1)
            act.wait_ge(s_w, 16 * 6)
            act.wait_ge(s_x, 16)
            with act.Fori(0, TURNS) as i:
                for u in range(UNITS):
                    if u == 0:
                        for v in range(UNITS):
                            act.wait_ge(s_et[(v + 1) * TPT - 1], i)
                        nc.scalar.copy(x_now[:], x_rows[:, bass.ds(i * UNITS, UNITS), :]).then_inc(s_xnow, 1)
                    for t in range(1, TPT, 2):
                        copy_tile(act, nc.scalar.copy, i, u, t)
                    act.wait_ge(s_h1p, i)
                    n = UNIT_B * FPG * len(gathers_of(TPT - 1))
                    nc.scalar.copy(xt[:, u * UNIT_B:(u + 1) * UNIT_B],
                                   p_et[(u * TPT + TPT - 1) % ET_BANKS][:, n:n + UNIT_B]).then_inc(s_xt[u], 1)
                    copy_z(act, nc.scalar.copy, i, u, range(1, QUADS, 2), s_z_act)
                act.wait_ge(s_h1p, i + 1)
                for n in range(N1 // 2, N1):
                    last = nc.scalar.activation(h1[:, n, :], p_h1[n], ACT.Relu, bias=b1_sb[:, n:n + 1])
                last.then_inc(s_h1_act, 1)
                act.wait_ge(s_h2p, i + 1)
                nc.scalar.activation(h2[:, 1, :], p_h2[1], ACT.Relu, bias=b2_sb[:, 1:2]).then_inc(s_h2_act, 1)

        @block.tensor
        def _(pe):
            pe.wait_ge(s_ident, 2)
            pe.wait_ge(s_w, 16 * 6)
            with pe.Fori(0, TURNS) as i:
                for u in range(UNITS):
                    pe.wait_ge(s_xnow, i + 1)
                    for t in range(TPT):
                        tile = u * TPT + t
                        before = (tile - ET_BANKS) % (UNITS * TPT)
                        pe.wait_ge(s_ct[before], i + 1 if before < tile else i)
                        if before % TPT == TPT - 1:
                            pe.wait_ge(s_xt[before // TPT], i + 1 if before < tile else i)
                        bank = p_et[tile % ET_BANKS]
                        for k, g in enumerate(gathers_of(t)):
                            slot = u * GATHERS + g
                            pe.wait_ge(s_row[slot], 16 * (i + 1))
                            last = nc.tensor.transpose(bank[:, k * P:(k + 1) * P], rows[:, slot, :], ident[:])
                        if t == TPT - 1:
                            k = len(gathers_of(t))
                            last = nc.tensor.transpose(bank[:, k * P:k * P + UNIT_B], x_now[:, u, :],
                                                       ident[0:UNIT_B, 0:UNIT_B])
                        last.then_inc(s_et[tile], 1)
                    for t in range(TPT):
                        pe.wait_ge(s_ct[u * TPT + t], i + 1)
                    pe.wait_ge(s_z_dve[u], i)
                    pe.wait_ge(s_z_act[u], i)
                    for b in range(CLASS_B):
                        for s in range(QUADS):
                            v = ct[:, u, s * CLASS_B + b, :]
                            last = nc.tensor.matmul(p_gram[u][QP * s:QP * (s + 1), b, :], v, v[:, 0:GW],
                                                    start=True, stop=True)
                    last.then_inc(s_gram[u], 1)
                for u in range(UNITS):
                    pe.wait_ge(s_z_dve[u], i + 1)
                    pe.wait_ge(s_z_act[u], i + 1)
                    pe.wait_ge(s_xt[u], i + 1)
                pe.wait_ge(s_h2_act, i)
                pe.wait_ge(s_y, i)
                for n in range(N1):
                    nc.tensor.matmul(p_h1[n], w1x_sb[:, n * P:(n + 1) * P], xt[:], start=True, stop=False)
                    for g in range(JB):
                        last = nc.tensor.matmul(p_h1[n], w1z_sb[:, g, n * P:(n + 1) * P], z[:, g, :],
                                                start=False, stop=(g == JB - 1))
                last.then_inc(s_h1p, 1)
                pe.wait_ge(s_h1_dve, i + 1)
                pe.wait_ge(s_h1_act, i + 1)
                for n in range(N2):
                    for k in range(N1):
                        last = nc.tensor.matmul(p_h2[n], w2_sb[:, k, n * P:(n + 1) * P], h1[:, k, :],
                                                start=(k == 0), stop=(k == N1 - 1))
                last.then_inc(s_h2p, 1)
                pe.wait_ge(s_h2_dve, i + 1)
                pe.wait_ge(s_h2_act, i + 1)
                for k in range(N2):
                    last = nc.tensor.matmul(p_y, w3_sb[:, k:k + 1], h2[:, k, :],
                                            start=(k == 0), stop=(k == N2 - 1))
                last.then_inc(s_yp, 1)


def kernel(**inputs):
    import concourse.bacc as bacc
    from concourse.bass_utils import run_bass_kernel_spmd

    a = {k: np.asarray(v) for k, v in inputs.items()}
    tables = [a[f"tbl_{f}"] for f in range(F)]
    starts = np.cumsum([0] + [t.shape[0] for t in tables[:-1]])
    ids = a["ids"].reshape(B // UNIT_B, UNIT_B, GATHERS, FPG).transpose(3, 1, 0, 2).reshape(P, TURNS * SLOTS)
    base = np.repeat(starts.reshape(GATHERS, FPG).T, UNIT_B, axis=0).astype(np.int32)
    pairs = np.full((NF + 1, NF), NF * (NF - 1) // 2)
    low, high = np.triu_indices(NF, k=1)
    pairs[high, low] = np.arange(len(low))
    rows = np.full((QUADS, QP, JB), NF * (NF - 1) // 2)
    rows[:, :NF, :] = pairs.reshape(QUADS, JB, NF).transpose(0, 2, 1)
    w1 = a["W_top1"]
    padded = np.concatenate([w1[:len(low)], np.zeros((1, H1), w1.dtype)])
    arrays = {
        "xt_rows": a["r_dense_x"].reshape(B // UNIT_B, UNIT_B, D).transpose(1, 0, 2),
        "ids": ids,
        "base": base,
        "table": np.concatenate(tables),
        "w1z": padded[rows.reshape(P, JB)],
        "w1x": w1[len(low):],
        "b1": a["b_top1"].reshape(N1, P).T,
        "w2": a["W_top2"].reshape(N1, P, H2).transpose(1, 0, 2),
        "b2": a["b_top2"].reshape(N2, P).T,
        "w3": a["W_top3"].reshape(N2, P).T,
    }
    arrays = {k: np.ascontiguousarray(v) for k, v in arrays.items()}

    nc = bacc.Bacc("TRN2", target_bir_lowering=False, num_devices=1)
    args = [nc.dram_tensor(k, v.shape, mybir.dt.from_np(v.dtype), kind="ExternalInput").ap() for k, v in arrays.items()]
    out = nc.dram_tensor("y", (1, B), mybir.dt.float32, kind="ExternalOutput").ap()
    interaction_kernel(nc, *args, out)
    r = run_bass_kernel_spmd(nc, [arrays], core_ids=[0])
    return r.results[0]["y"].reshape(B, 1)
```

```python
import numpy as np
import concourse.bass as bass
from concourse import mybir
from contextlib import ExitStack

B = 512
D = 128
F = 26
NF = F + 1
PAIRS = NF * (NF - 1) // 2
H1, H2 = 512, 256
P = 128
QP = 32
QUADS = P // QP

PICKED = [5, 6, 11, 12]
GATHERED = [f for f in range(F) if f not in PICKED]
VECTORS = GATHERED + [F] + PICKED
PICKED_ROWS = 1000
PICK_K = 8
PICK_P = PICKED_ROWS // PICK_K

TILE_B = 128
TURNS = B // TILE_B
UNIT_B = 64
UNITS = TILE_B // UNIT_B
FPG = P // UNIT_B
GATHERS = len(GATHERED) // FPG
SLOTS = UNITS * GATHERS
GPT = 4
TPT = -(-GATHERS // GPT)
TILES = UNITS * TPT
ET_BANKS = 2
HALF = len(PICKED) // 2
CLASS_B = UNIT_B // QUADS
GW = 28
JB = GW // QUADS
N1 = H1 // P
N2 = H2 // P
LAST = TURNS - 1
ZEROED = 2


def interaction_kernel(nc, x, ids, base, picked_ids, picked_row, picked_tables, table, w1z, w1x, b1, w2, b2, w3, out):
    fp32 = mybir.dt.float32
    bf16 = mybir.dt.bfloat16
    fp16 = mybir.dt.float16
    i32 = mybir.dt.int32
    ALU = mybir.AluOpType
    ACT = mybir.ActivationFunctionType

    ctx = ExitStack()
    with ctx:
        def sb(name, shape, dt=fp32):
            return ctx.enter_context(nc.sbuf_tensor(name, shape, dt))

        def pb(name, shape):
            return ctx.enter_context(nc.psum_tensor(name, shape, fp32))

        def sem(name):
            return ctx.enter_context(nc.semaphore(name))

        ids_sb = sb("ids_sb", [P, TURNS * SLOTS], i32)
        base_sb = sb("base_sb", [P, GATHERS], i32)
        idx_all = sb("idx_all", [P, (TURNS + 1) * SLOTS], i32)
        idx_now = sb("idx_now", [P, UNITS, GATHERS], i32)
        rows = sb("rows", [P, SLOTS, D])
        pid_i = sb("pid_i", [PICK_P, TURNS, len(PICKED) * TILE_B], i32)
        pid = sb("pid", [PICK_P, TURNS + 1, len(PICKED) * TILE_B], fp16)
        prow = sb("prow", [PICK_P, PICK_K])
        tab = [sb(f"tab{k}", [PICK_P, PICK_K, D]) for k in range(len(PICKED))]
        res = [sb(f"res{k}", [PICK_P, PICK_K, D]) for k in range(len(PICKED))]
        low = [sb(f"low{k}", [PICK_P, PICK_K, D], bf16) for k in range(len(PICKED))]
        onehot = [sb(f"onehot{k}", [PICK_P, PICK_K, TILE_B], bf16) for k in range(len(PICKED))]
        picked = sb("picked", [P, len(PICKED), TILE_B])
        x_rows = sb("x_rows", [P, B // P, D])
        xt = sb("xt", [P, B])
        ident = sb("ident", [P, P])
        ct = sb("ct", [P, UNITS, UNIT_B, QP])
        z = sb("z", [P, JB, TILE_B])
        w1z_sb = sb("w1z_sb", [P, JB, H1])
        w1x_sb = sb("w1x_sb", [D, H1])
        w2_sb = sb("w2_sb", [P, N1, H2])
        w3_sb = sb("w3_sb", [P, N2])
        b1_sb = sb("b1_sb", [P, N1])
        b2_sb = sb("b2_sb", [P, N2])
        h1 = sb("h1", [P, N1, TILE_B])
        h2 = sb("h2", [P, N2, TILE_B])
        y_sb = sb("y_sb", [1, B])

        p_et = [pb(f"p_et{k}", [P, 512]) for k in range(ET_BANKS)]
        p_gram = [pb(f"p_gram{u}", [P, CLASS_B, GW]) for u in range(UNITS)]
        p_pick = pb("p_pick", [P, len(PICKED), TILE_B])
        p_mlp = [pb(f"p_mlp{k}", [P, 4, TILE_B]) for k in range(3)]
        p_h1 = [p_mlp[n * 2 // N1][:, n % (N1 // 2), :] for n in range(N1)]
        p_h2 = [p_mlp[2][:, 0, :], p_mlp[0][:, 2, :]]
        p_y = p_mlp[2][0:1, 1, :]

        s_ids = sem("s_ids")
        s_prow = sem("s_prow")
        s_pid = [sem(f"s_pid{t}") for t in range(TURNS)]
        s_tab = [sem(f"s_tab{k}") for k in range(len(PICKED))]
        s_x = sem("s_x")
        s_w = sem("s_w")
        s_idx_all = sem("s_idx_all")
        s_idx = [sem(f"s_idx{u}") for u in range(UNITS)]
        s_units = sem("s_units")
        s_row = [sem(f"s_row{g}") for g in range(SLOTS)]
        s_ident = sem("s_ident")
        s_zero = sem("s_zero")
        s_pid16_0 = sem("s_pid16_0")
        s_pid16 = sem("s_pid16")
        s_res = [sem(f"s_res{k}") for k in range(len(PICKED))]
        s_low = [sem(f"s_low{k}") for k in range(len(PICKED))]
        s_xp = sem("s_xp")
        s_xt = sem("s_xt")
        s_onehot = [sem(f"s_onehot{k}") for k in range(len(PICKED))]
        s_picked = [sem(f"s_picked{k}") for k in range(len(PICKED))]
        s_stage = [sem(f"s_stage{h}") for h in range(2)]
        s_et = [sem(f"s_et{t}") for t in range(TILES)]
        s_ct = [sem(f"s_ct{t}") for t in range(TILES)]
        s_cx = [sem(f"s_cx{u}") for u in range(UNITS)]
        s_gram = [sem(f"s_gram{u}") for u in range(UNITS)]
        s_z_dve = [sem(f"s_z_dve{u}") for u in range(UNITS)]
        s_z_act = [sem(f"s_z_act{u}") for u in range(UNITS)]
        s_h1p = [sem(f"s_h1p{k}") for k in range(2)]
        s_h1_dve = sem("s_h1_dve")
        s_h1_act = sem("s_h1_act")
        s_h2p = sem("s_h2p")
        s_h2_dve = sem("s_h2_dve")
        s_h2_act = sem("s_h2_act")
        s_yp = sem("s_yp")
        s_y = sem("s_y")
        s_out = sem("s_out")

        block = ctx.enter_context(nc.Block())

        def done(i):
            return i + 2

        def gathers_of(t):
            return range(t * GPT, min((t + 1) * GPT, GATHERS))

        def samples(i):
            return bass.ds(i * TILE_B, TILE_B)

        def top_half(t):
            return t[:].bitcast(bf16).rearrange("p k (d h) -> p k d h", h=2)[:, :, :, 1]

        def one_turn(t, i):
            return t[:, i, :] if isinstance(i, int) else t[:, bass.ds(i, 1), :].rearrange("p a n -> p (a n)")

        def copy_tile(engine, copy, i, u, t):
            tile = u * TPT + t
            engine.wait_ge(s_gram[u], done(i - 1))
            engine.wait_ge(s_et[tile], done(i))
            f0, n = t * GPT * FPG, FPG * len(gathers_of(t))
            src = p_et[tile % ET_BANKS][:, 0:n * UNIT_B].rearrange("p (f s) -> p s f", s=UNIT_B)
            copy(ct[:, u, :, f0:f0 + n], src).then_inc(s_ct[tile], 1)

        def copy_z(engine, copy, i, u, classes, finished):
            engine.wait_ge(s_gram[u], done(i))
            engine.wait_ge(s_h1p[0], done(i - 1))
            for s in classes:
                for j in range(QUADS):
                    b0 = u * UNIT_B + s * CLASS_B
                    last = copy(z[QP * j:QP * (j + 1), :, b0:b0 + CLASS_B],
                                p_gram[u][QP * s:QP * (s + 1), :, JB * j:JB * (j + 1)].rearrange("p b g -> p g b"))
            last.then_inc(finished[u], 1)

        @block.sync
        def _(sp):
            sp.dma_start(ids_sb[:], ids).then_inc(s_ids, 16)
            for k in range(len(PICKED)):
                sp.dma_start(tab[k][:], picked_tables[k]).then_inc(s_tab[k], 16)
                if k == 0:
                    sp.dma_start(x_rows[:], x).then_inc(s_x, 16)
            for t in range(1, TURNS):
                sp.dma_start(pid_i[:, t, :], picked_ids[t:t + 1, :].broadcast_to([PICK_P, len(PICKED) * TILE_B]))\
                    .then_inc(s_pid[t], 16)
            sp.dma_start(w1x_sb[:], w1x).then_inc(s_w, 16)
            sp.dma_start(w1z_sb[:], w1z).then_inc(s_w, 16)
            sp.dma_start(w2_sb[:], w2).then_inc(s_w, 16)
            sp.dma_start(w3_sb[:], w3).then_inc(s_w, 16)
            sp.dma_start(b1_sb[:], b1).then_inc(s_w, 16)
            sp.dma_start(b2_sb[:], b2).then_inc(s_w, 16)
            sp.wait_ge(s_y, done(LAST))
            sp.dma_start(out, y_sb[:]).then_inc(s_out, 16)
            sp.wait_ge(s_out, 16)

        @block.gpsimd
        def _(pool):
            nc.gpsimd.memset(ident[:], 0.0).then_inc(s_ident, 1)
            pool.wait_ge(s_ident, 1)
            nc.gpsimd.affine_select(out=ident[:], in_=ident[:], compare_op=ALU.not_equal, fill=1.0, base=0,
                                    pattern=[[-1, P]], channel_multiplier=1).then_inc(s_ident, 1)
            with pool.Fori(0, TURNS) as i:
                for u in range(UNITS):
                    pool.wait_ge(s_idx[u], i + 1)
                    pool.sem_inc(s_units, 1)
                    for g in range(GATHERS):
                        slot = u * GATHERS + g
                        pool.indirect_dma_start(
                            out=rows[:, slot, :], out_offset=None, in_=table,
                            in_offset=bass.IndirectOffsetOnAxis(ap=idx_now[:, u, g:g + 1], axis=0),
                        ).then_inc(s_row[slot], 16)

        @block.vector
        def _(dve):
            nc.vector.memset(idx_all[:, TURNS * SLOTS:], 0).then_inc(s_idx_all, 1)
            dve.wait_ge(s_ids, 32)
            nc.vector.tensor_tensor(
                idx_all[:, 0:TURNS * SLOTS].rearrange("p (v g) -> p v g", g=GATHERS),
                ids_sb[:].rearrange("p (v g) -> p v g", g=GATHERS),
                base_sb[:].rearrange("p (a g) -> p a g", a=1).broadcast_to([P, TURNS * UNITS, GATHERS]),
                ALU.add).then_inc(s_idx_all, 1)
            dve.wait_ge(s_idx_all, 2)
            for u in range(UNITS):
                nc.vector.tensor_copy(idx_now[:, u, :], idx_all[:, u * GATHERS:(u + 1) * GATHERS]).then_inc(s_idx[u], 1)
            nc.vector.memset(ct[:, :, :, NF:QP], 0.0).then_inc(s_zero, 1)
            nc.vector.memset(pid[:, TURNS, :], 0.0).then_inc(s_zero, 1)
            for s in [*s_ct[0::2], *s_z_dve, s_y, s_h1_dve, s_h2_dve]:
                dve.sem_inc(s, 1)

            def one_hot(i, tables):
                for k in tables:
                    now = slice(k * TILE_B, (k + 1) * TILE_B)
                    for c in range(PICK_K):
                        last = nc.vector.tensor_scalar(onehot[k][:, c, :], one_turn(pid, i)[:, now], prow[:, c:c + 1],
                                                       None, ALU.is_equal)
                    last.then_inc(s_onehot[k], 1)

            dve.wait_ge(s_pid[0], 16)
            nc.vector.tensor_copy(pid[:, 0, :], pid_i[:, 0, :]).then_inc(s_pid16_0, 1)
            dve.wait_ge(s_prow, 16)
            dve.wait_ge(s_pid16_0, 1)
            for k in range(len(PICKED)):
                one_hot(0, [k])
                dve.wait_ge(s_tab[k], 16)
                nc.vector.tensor_tensor(res[k][:], tab[k][:], top_half(tab[k]), ALU.subtract).then_inc(s_res[k], 1)
                dve.wait_ge(s_res[k], 1)
                nc.vector.tensor_tensor(low[k][:], res[k][:], top_half(res[k]), ALU.subtract).then_inc(s_low[k], 1)

            def relu_h1(i):
                dve.wait_ge(s_h2p, done(i - 1))
                dve.wait_ge(s_h1p[0], done(i))
                for n in range(N1 // 2):
                    last = nc.vector.tensor_scalar(h1[:, n, :], p_h1[n], b1_sb[:, n:n + 1], 0.0, ALU.add, ALU.max)
                last.then_inc(s_h1_dve, 1)

            def relu_h2(i):
                dve.wait_ge(s_yp, done(i - 1))
                dve.wait_ge(s_h2p, done(i))
                nc.vector.tensor_scalar(h2[:, 0, :], p_h2[0], b2_sb[:, 0:1], 0.0, ALU.add, ALU.max)\
                    .then_inc(s_h2_dve, 1)

            def copy_y(i):
                dve.wait_ge(s_yp, done(i))
                nc.vector.tensor_copy(y_sb[0:1, samples(i)], p_y).then_inc(s_y, 1)

            def tile(i, u, t):
                copy_tile(dve, nc.vector.tensor_copy, i, u, t)

            def next_indices(i, u):
                for t in range(TPT):
                    dve.wait_ge(s_et[u * TPT + t], done(i - 1))
                nc.vector.tensor_copy(idx_now[:, u, :], idx_all[:, bass.ds(i * SLOTS + u * GATHERS, GATHERS)])\
                    .then_inc(s_idx[u], 1)

            def products(i, u):
                copy_z(dve, nc.vector.tensor_copy, i, u, range(0, QUADS, 2), s_z_dve)

            def next_one_hot(i, tables):
                for k in tables:
                    dve.wait_ge(s_picked[k], i)
                    one_hot(i, [k])

            dve.wait_ge(s_zero, ZEROED)
            tile(0, 0, 0)
            tile(0, 0, 2)
            next_indices(1, 0)
            dve.wait_ge(s_pid16, TURNS - 1)
            next_one_hot(1, range(HALF))
            products(0, 0)
            tile(0, 1, 1)
            next_one_hot(1, range(HALF, len(PICKED)))
            dve.wait_ge(s_w, 16 * 6)
            with dve.Fori(0, LAST) as i:
                next_indices(i + 1, 1)
                products(i, 1)
                next_one_hot(i + 2, [0])
                tile(i + 1, 0, 0)
                tile(i + 1, 0, 2)
                next_indices(i + 2, 0)
                next_one_hot(i + 2, range(1, len(PICKED)))
                relu_h1(i)
                products(i + 1, 0)
                relu_h2(i)
                tile(i + 1, 1, 1)
                copy_y(i)
            products(LAST, 1)
            relu_h1(LAST)
            relu_h2(LAST)
            copy_y(LAST)

        @block.scalar
        def _(act):
            act.dma_start(base_sb[:], base).then_inc(s_ids, 16)
            act.dma_start(pid_i[:, 0, :], picked_ids[0:1, :].broadcast_to([PICK_P, len(PICKED) * TILE_B]))\
                .then_inc(s_pid[0], 16)
            act.dma_start(prow[:], picked_row).then_inc(s_prow, 16)
            for s in [*s_ct[1::2], *s_cx, *s_z_act, s_h1_act, s_h2_act]:
                act.sem_inc(s, 1)

            def narrow_ids(i):
                act.wait_ge(s_pid[i], 16)
                nc.scalar.copy(pid[:, i, :], pid_i[:, i, :]).then_inc(s_pid16, 1)

            def stage(i, h):
                ks = slice(h * HALF, (h + 1) * HALF)
                for k in range(h * HALF, (h + 1) * HALF):
                    act.wait_ge(s_picked[k], i + 1)
                for u in range(UNITS):
                    act.wait_ge(s_cx[u], done(i - 1))
                nc.scalar.copy(picked[:, ks, :], p_pick[:, ks, :]).then_inc(s_stage[h], 1)

            def columns(i, u):
                act.wait_ge(s_gram[u], done(i - 1))
                for h in range(2):
                    act.wait_ge(s_stage[h], i + 1)
                nc.scalar.copy(ct[:, u, :, len(GATHERED)], xt[:, bass.ds(i * TILE_B + u * UNIT_B, UNIT_B)])
                nc.scalar.copy(ct[:, u, :, len(GATHERED) + 1:NF],
                               picked[:, :, u * UNIT_B:(u + 1) * UNIT_B].rearrange("p v s -> p s v"))\
                    .then_inc(s_cx[u], 1)

            def relu_h1(i):
                act.wait_ge(s_h2p, done(i - 1))
                act.wait_ge(s_h1p[1], done(i))
                for n in range(N1 // 2, N1):
                    last = nc.scalar.activation(h1[:, n, :], p_h1[n], ACT.Relu, bias=b1_sb[:, n:n + 1])
                last.then_inc(s_h1_act, 1)

            def relu_h2(i):
                act.wait_ge(s_yp, done(i - 1))
                act.wait_ge(s_h2p, done(i))
                nc.scalar.activation(h2[:, 1, :], p_h2[1], ACT.Relu, bias=b2_sb[:, 1:2]).then_inc(s_h2_act, 1)

            def tile(i, u, t):
                copy_tile(act, nc.scalar.copy, i, u, t)

            def products(i, u):
                copy_z(act, nc.scalar.copy, i, u, range(1, QUADS, 2), s_z_act)

            act.wait_ge(s_xp, 1)
            nc.scalar.copy(xt[:], p_mlp[2][:].rearrange("p n b -> p (n b)")).then_inc(s_xt, 1)
            for t in range(1, TURNS):
                narrow_ids(t)
            act.wait_ge(s_zero, ZEROED)
            act.wait_ge(s_xt, 1)
            stage(0, 0)
            stage(0, 1)
            for u in range(UNITS):
                columns(0, u)
            tile(0, 0, 1)
            products(0, 0)
            tile(0, 1, 0)
            act.wait_ge(s_w, 16 * 6)
            with act.Fori(0, LAST) as i:
                tile(i, 1, 2)
                stage(i + 1, 0)
                products(i, 1)
                stage(i + 1, 1)
                for u in range(UNITS):
                    columns(i + 1, u)
                tile(i + 1, 0, 1)
                relu_h1(i)
                products(i + 1, 0)
                relu_h2(i)
                tile(i + 1, 1, 0)
            tile(LAST, 1, 2)
            products(LAST, 1)
            relu_h1(LAST)
            relu_h2(LAST)

        @block.tensor
        def _(pe):
            for s in [*s_et, *s_gram, *s_h1p, s_h2p, s_yp]:
                pe.sem_inc(s, 1)

            def pick(i, tables):
                for k in tables:
                    if k >= HALF:
                        pe.wait_ge(s_stage[0], i + 1)
                    elif not isinstance(i, int):
                        pe.wait_ge(s_stage[1], i)
                    pe.wait_ge(s_onehot[k], i + 1)
                    for n, part in enumerate((top_half(tab[k]), top_half(res[k]), low[k])):
                        if isinstance(i, int):
                            pe.wait_ge((s_tab[k], s_res[k], s_low[k])[n], (16, 1, 1)[n])
                        for c in range(PICK_K):
                            last = nc.tensor.matmul(p_pick[:, k, :], part[:, c, :], onehot[k][:, c, :],
                                                    start=(n == 0 and c == 0), stop=(n == 2 and c == PICK_K - 1))
                    last.then_inc(s_picked[k], 1)

            def transposes(i, u, tiles):
                for t in tiles:
                    tile = u * TPT + t
                    before = (tile - ET_BANKS) % TILES
                    pe.wait_ge(s_ct[before], done(i) if before < tile else done(i - 1))
                    for k, g in enumerate(gathers_of(t)):
                        slot = u * GATHERS + g
                        pe.wait_ge(s_row[slot], 16 * (i + 1))
                        last = nc.tensor.transpose(p_et[tile % ET_BANKS][:, k * P:(k + 1) * P], rows[:, slot, :],
                                                   ident[:])
                    last.then_inc(s_et[tile], 1)

            def products(i, u):
                for t in range(TPT):
                    pe.wait_ge(s_ct[u * TPT + t], done(i))
                pe.wait_ge(s_cx[u], done(i))
                pe.wait_ge(s_z_dve[u], done(i - 1))
                pe.wait_ge(s_z_act[u], done(i - 1))
                for b in range(CLASS_B):
                    for s in range(QUADS):
                        v = ct[:, u, s * CLASS_B + b, :]
                        last = nc.tensor.matmul(p_gram[u][QP * s:QP * (s + 1), b, :], v, v[:, 0:GW],
                                                start=True, stop=True)
                last.then_inc(s_gram[u], 1)

            def layer1(i, half):
                pe.wait_ge((s_h1_dve, s_h1_act)[half], done(i - 1))
                if half == 0:
                    pe.wait_ge(s_h2_act, done(i - 1))
                for n in range(half * N1 // 2, (half + 1) * N1 // 2):
                    nc.tensor.matmul(p_h1[n], w1x_sb[:, n * P:(n + 1) * P], xt[:, samples(i)], start=True, stop=False)
                    if half == 1 and n == N1 // 2:
                        for u in range(UNITS):
                            pe.wait_ge(s_z_dve[u], done(i))
                            pe.wait_ge(s_z_act[u], done(i))
                    for g in range(JB):
                        last = nc.tensor.matmul(p_h1[n], w1z_sb[:, g, n * P:(n + 1) * P], z[:, g, :],
                                                start=False, stop=(g == JB - 1))
                last.then_inc(s_h1p[half], 1)

            def layer2(i):
                pe.wait_ge(s_y, done(i - 1))
                pe.wait_ge(s_h1_dve, done(i))
                pe.wait_ge(s_h1_act, done(i))
                for n in range(N2):
                    for k in range(N1):
                        last = nc.tensor.matmul(p_h2[n], w2_sb[:, k, n * P:(n + 1) * P], h1[:, k, :],
                                                start=(k == 0), stop=(k == N1 - 1))
                last.then_inc(s_h2p, 1)

            def layer3(i):
                pe.wait_ge(s_h2_dve, done(i))
                pe.wait_ge(s_h2_act, done(i))
                for k in range(N2):
                    last = nc.tensor.matmul(p_y, w3_sb[:, k:k + 1], h2[:, k, :], start=(k == 0), stop=(k == N2 - 1))
                last.then_inc(s_yp, 1)

            pe.wait_ge(s_ident, 2)
            pe.wait_ge(s_x, 16)
            for t in range(B // P):
                last = nc.tensor.transpose(p_mlp[2][:, t, :], x_rows[:, t, :], ident[:])
            last.then_inc(s_xp, 1)
            pick(0, range(len(PICKED)))
            transposes(0, 0, range(TPT))
            pe.wait_ge(s_xt, 1)
            pe.wait_ge(s_w, 16 * 6)
            pe.wait_ge(s_zero, ZEROED)
            products(0, 0)
            transposes(0, 1, range(TPT - 1))
            with pe.Fori(0, LAST) as i:
                pick(i + 1, [0])
                transposes(i, 1, [TPT - 1])
                pick(i + 1, [1])
                products(i, 1)
                pick(i + 1, range(HALF, len(PICKED)))
                transposes(i + 1, 0, range(TPT - 1))
                layer1(i, 1)
                transposes(i + 1, 0, [TPT - 1])
                layer1(i, 0)
                products(i + 1, 0)
                layer2(i)
                transposes(i + 1, 1, range(TPT - 1))
                layer3(i)
            transposes(LAST, 1, [TPT - 1])
            products(LAST, 1)
            layer1(LAST, 1)
            layer1(LAST, 0)
            layer2(LAST)
            layer3(LAST)


def kernel(**inputs):
    import concourse.bacc as bacc
    from concourse.bass_utils import run_bass_kernel_spmd

    a = {k: np.asarray(v) for k, v in inputs.items()}
    tables = [a[f"tbl_{f}"] for f in GATHERED]
    starts = np.cumsum([0] + [t.shape[0] for t in tables[:-1]])
    ids = a["ids"][:, GATHERED].reshape(B // UNIT_B, UNIT_B, GATHERS, FPG).transpose(3, 1, 0, 2)
    base = np.repeat(starts.reshape(GATHERS, FPG).T, UNIT_B, axis=0).astype(np.int32)
    low, high = np.triu_indices(NF, k=1)
    pair = np.full((NF, NF), PAIRS)
    pair[low, high] = pair[high, low] = np.arange(PAIRS)
    rows = np.full((QUADS, QP, JB), PAIRS)
    for f in range(NF):
        for g in range(f + 1, NF):
            rows[g // JB, f, g % JB] = pair[VECTORS[f], VECTORS[g]]
    w1 = a["W_top1"]
    padded = np.concatenate([w1[:PAIRS], np.zeros((1, H1), w1.dtype)])
    arrays = {
        "x": a["r_dense_x"].reshape(B // P, P, D).transpose(1, 0, 2),
        "ids": ids.reshape(P, TURNS * SLOTS),
        "base": base,
        "picked_ids": a["ids"][:, PICKED].reshape(TURNS, TILE_B, len(PICKED)).transpose(0, 2, 1).reshape(TURNS, -1),
        "picked_row": np.arange(PICKED_ROWS, dtype=np.float32).reshape(PICK_P, PICK_K),
        "picked_tables": np.stack([a[f"tbl_{f}"].reshape(PICK_P, PICK_K, D) for f in PICKED]),
        "table": np.concatenate(tables),
        "w1z": padded[rows.reshape(P, JB)],
        "w1x": w1[PAIRS:],
        "b1": a["b_top1"].reshape(N1, P).T,
        "w2": a["W_top2"].reshape(N1, P, H2).transpose(1, 0, 2),
        "b2": a["b_top2"].reshape(N2, P).T,
        "w3": a["W_top3"].reshape(N2, P).T,
    }
    arrays = {k: np.ascontiguousarray(v) for k, v in arrays.items()}

    nc = bacc.Bacc("TRN2", target_bir_lowering=False, num_devices=1)
    args = [nc.dram_tensor(k, v.shape, mybir.dt.from_np(v.dtype), kind="ExternalInput").ap() for k, v in arrays.items()]
    out = nc.dram_tensor("y", (1, B), mybir.dt.float32, kind="ExternalOutput").ap()
    interaction_kernel(nc, *args, out)
    r = run_bass_kernel_spmd(nc, [arrays], core_ids=[0])
    return r.results[0]["y"].reshape(B, 1)
```

```python
import numpy as np
import concourse.bass as bass
from concourse import mybir
from contextlib import ExitStack

B = 512
D = 128
F = 26
NF = F + 1
PAIRS = NF * (NF - 1) // 2
H1, H2 = 512, 256
P = 128
QP = 32
QUADS = P // QP

PICKED = [5, 6, 11, 12]
PICKED_ENDS = [16, 17]
PICKED_ALL = PICKED + PICKED_ENDS
GATHERED = PICKED_ENDS + [f for f in range(F) if f not in PICKED_ALL]
VECTORS = GATHERED + [F] + PICKED
PICKED_ROWS = 1000
PICK_K = 8
PICK_P = PICKED_ROWS // PICK_K

TILE_B = 128
TURNS = B // TILE_B
UNIT_B = 64
UNITS = TILE_B // UNIT_B
FPG = P // UNIT_B
GATHERS = len(GATHERED) // FPG
SLOTS = UNITS * GATHERS
GPT = 4
TPT = -(-GATHERS // GPT)
TILES = UNITS * TPT
ET_BANKS = 2
SKIPPED = len(PICKED_ENDS) // FPG
HALF = len(PICKED) // 2
CLASS_B = UNIT_B // QUADS
GW = 28
JB = GW // QUADS
N1 = H1 // P
N2 = H2 // P
LAST = TURNS - 1
LOADS = JB + 5
WARM_UP = 20
WARM_PRODUCTS = 9
WARM_ROW = 2


def interaction_kernel(nc, x, ids, picked_ids_0, picked_ids, picked_ids_last, picked_row, picked_tables, table, w1z,
                       w1x, b1, w2, b2, w3, out):
    fp32 = mybir.dt.float32
    bf16 = mybir.dt.bfloat16
    fp16 = mybir.dt.float16
    i32 = mybir.dt.int32
    ALU = mybir.AluOpType
    ACT = mybir.ActivationFunctionType

    ctx = ExitStack()
    with ctx:
        def sb(name, shape, dt=fp32):
            return ctx.enter_context(nc.sbuf_tensor(name, shape, dt))

        def pb(name, shape):
            return ctx.enter_context(nc.psum_tensor(name, shape, fp32))

        def sem(name):
            return ctx.enter_context(nc.semaphore(name))

        ids_sb = sb("ids_sb", [P, GATHERS + TURNS * SLOTS], i32)
        idx_all = sb("idx_all", [P, LAST * SLOTS], i32)
        idx_now = sb("idx_now", [P, UNITS, GATHERS], i32)
        rows = sb("rows", [P, SLOTS, D])
        pid_0 = sb("pid_0", [PICK_P, len(PICKED_ALL), TILE_B], i32)
        pid_i = sb("pid_i", [PICK_P, LAST, len(PICKED) * TILE_B], i32)
        pid = sb("pid", [PICK_P, LAST, len(PICKED) * TILE_B], fp16)
        pid_last = sb("pid_last", [PICK_P, len(PICKED_ENDS), TILE_B], i32)
        prow = sb("prow", [PICK_P, PICK_K])
        tab = [sb(f"tab{k}", [PICK_P, PICK_K, D]) for k in range(len(PICKED_ALL))]
        res = [sb(f"res{k}", [PICK_P, PICK_K, D]) for k in range(len(PICKED_ALL))]
        low = [sb(f"low{k}", [PICK_P, PICK_K, D], bf16) for k in range(len(PICKED_ALL))]
        onehot = [sb(f"onehot{k}", [PICK_P, PICK_K, TILE_B], bf16) for k in range(len(PICKED_ALL))]
        onehot_0 = [sb(f"onehot_0{k}", [PICK_P, PICK_K, TILE_B]) for k in range(len(PICKED_ALL))]
        picked = sb("picked", [P, len(PICKED), TILE_B])
        x_rows = sb("x_rows", [P, B // P, D])
        xt = sb("xt", [P, B])
        ident = sb("ident", [P, P])
        ct = sb("ct", [P, UNITS, UNIT_B, QP])
        z = sb("z", [P, JB, TILE_B])
        w1z_sb = sb("w1z_sb", [P, JB, H1])
        w1x_sb = sb("w1x_sb", [D, H1])
        w2_sb = sb("w2_sb", [P, N1, H2])
        w3_sb = sb("w3_sb", [P, N2])
        b1_sb = sb("b1_sb", [P, N1])
        b2_sb = sb("b2_sb", [P, N2])
        h1 = sb("h1", [P, N1, TILE_B])
        h2 = sb("h2", [P, N2, TILE_B])
        y_sb = sb("y_sb", [1, B])

        p_et = [pb(f"p_et{k}", [P, 512]) for k in range(ET_BANKS)]
        p_gram = [pb(f"p_gram{u}", [P, CLASS_B, GW]) for u in range(UNITS)]
        p_pick = pb("p_pick", [P, len(PICKED), TILE_B])
        p_mlp = [pb(f"p_mlp{k}", [P, 4, TILE_B]) for k in range(3)]
        p_pick_0 = [p_pick[:, 0:HALF, :], p_mlp[0][:, 0:HALF, :], p_mlp[1][:, 0:len(PICKED_ENDS), :]]
        p_warm = p_gram[1][:].rearrange("p b g -> p (b g)")[:, 0:P]
        p_h1 = [p_mlp[n * 2 // N1][:, n % (N1 // 2), :] for n in range(N1)]
        p_h2 = [p_mlp[2][:, 0, :], p_mlp[0][:, 2, :]]
        p_y = p_mlp[2][0:1, 1, :]
        last_h1 = [p_mlp[1][:, 0, :], p_pick[:, 0, :], p_et[0][:, 0:TILE_B], p_et[1][:, 0:TILE_B]]

        s_ids = sem("s_ids")
        s_ids_later = sem("s_ids_later")
        s_prow = sem("s_prow")
        s_pid = [sem(f"s_pid{t}") for t in range(TURNS)]
        s_tab = [sem(f"s_tab{k}") for k in range(len(PICKED_ALL))]
        s_x = sem("s_x")
        s_w = sem("s_w")
        s_idx_all = sem("s_idx_all")
        s_idx = [sem(f"s_idx{u}") for u in range(UNITS)]
        s_units = sem("s_units")
        s_row = [sem(f"s_row{g}") for g in range(SLOTS)]
        s_ident = sem("s_ident")
        s_zero = sem("s_zero")
        s_zero_z = sem("s_zero_z")
        s_pid16 = sem("s_pid16")
        s_res = [sem(f"s_res{k}") for k in range(len(PICKED_ALL))]
        s_low = [sem(f"s_low{k}") for k in range(len(PICKED_ALL))]
        s_xp = sem("s_xp")
        s_xt = sem("s_xt")
        s_onehot_0 = [sem(f"s_onehot_0{k}") for k in range(len(PICKED_ALL))]
        s_onehot = [sem(f"s_onehot{k}") for k in range(len(PICKED))]
        s_picked = [sem(f"s_picked{k}") for k in range(len(PICKED_ALL))]
        s_stage = [sem(f"s_stage{h}") for h in range(2)]
        s_et = [sem(f"s_et{t}") for t in range(TILES)]
        s_ct = [sem(f"s_ct{t}") for t in range(TILES)]
        s_cx = [sem(f"s_cx{u}") for u in range(UNITS)]
        s_gram = [sem(f"s_gram{u}") for u in range(UNITS)]
        s_z_dve = [sem(f"s_z_dve{u}") for u in range(UNITS)]
        s_z_act = [sem(f"s_z_act{u}") for u in range(UNITS)]
        s_h1p = [sem(f"s_h1p{k}") for k in range(2)]
        s_h1_dve = sem("s_h1_dve")
        s_h1_act = sem("s_h1_act")
        s_h2p = sem("s_h2p")
        s_h2_dve = sem("s_h2_dve")
        s_h2_act = sem("s_h2_act")
        s_yp = sem("s_yp")
        s_y = sem("s_y")
        s_pid_last = sem("s_pid_last")
        s_last_onehot = [sem(f"s_last_onehot{k}") for k in range(len(PICKED_ENDS))]
        s_last_picked = sem("s_last_picked")
        s_last_columns = [sem(f"s_last_columns{u}") for u in range(UNITS)]
        s_last_gram = [sem(f"s_last_gram{h}") for h in range(2)]
        s_last_z_dve = sem("s_last_z_dve")
        s_last_z_act = sem("s_last_z_act")
        s_last_h1p = [sem(f"s_last_h1p{n}") for n in range(N1)]
        s_last_h1 = [sem(f"s_last_h1{n}") for n in range(N1)]
        s_last_h2p = [sem(f"s_last_h2p{n}") for n in range(N2)]
        s_out = sem("s_out")

        block = ctx.enter_context(nc.Block())

        def done(i):
            return i + 2

        def gathers_of(t):
            return range(t * GPT, min((t + 1) * GPT, GATHERS))

        def skipped(i, t):
            return SKIPPED if isinstance(i, int) and i in (0, LAST) and t == 0 else 0

        def samples(i):
            return bass.ds(i * TILE_B, TILE_B)

        def top_half(t):
            return t[:].bitcast(bf16).rearrange("p k (d h) -> p k d h", h=2)[:, :, :, 1]

        def one_turn(t, i):
            return t[:, i, :] if isinstance(i, int) else t[:, bass.ds(i, 1), :].rearrange("p a n -> p (a n)")

        def copy_tile(engine, copy, i, u, t):
            tile = u * TPT + t
            engine.wait_ge(s_gram[u], done(i - 1))
            engine.wait_ge(s_et[tile], done(i))
            f0, n, skip = t * GPT * FPG, FPG * len(gathers_of(t)), FPG * skipped(i, t)
            src = p_et[tile % ET_BANKS][:, skip * UNIT_B:n * UNIT_B].rearrange("p (f s) -> p s f", s=UNIT_B)
            copy(ct[:, u, :, f0 + skip:f0 + n], src).then_inc(s_ct[tile], 1)

        def copy_z(engine, copy, i, u, classes, finished):
            engine.wait_ge(s_gram[u], done(i))
            engine.wait_ge(s_h1p[0], done(i - 1))
            for s in classes:
                for j in range(QUADS):
                    b0 = u * UNIT_B + s * CLASS_B
                    last = copy(z[QP * j:QP * j + NF, :, b0:b0 + CLASS_B],
                                p_gram[u][QP * s:QP * s + NF, :, JB * j:JB * (j + 1)].rearrange("p b g -> p g b"))
            last.then_inc(finished[u], 1)

        def copy_last_z(engine, copy, classes, finished):
            for h in range(2):
                engine.wait_ge(s_last_gram[h], 1)
                for s in classes:
                    for j in range(QUADS):
                        b0 = (UNITS - 1) * UNIT_B + s * CLASS_B + h * CLASS_B // 2
                        last = copy(z[QP * j:QP * j + NF, :, b0:b0 + CLASS_B // 2],
                                    p_gram[1 - h][QP * s:QP * s + NF, 0:CLASS_B // 2, JB * j:JB * (j + 1)]
                                    .rearrange("p b g -> p g b"))
            last.then_inc(finished, 1)

        @block.sync
        def _(sp):
            first = GATHERS + SLOTS
            sp.dma_start(ids_sb[:, 0:first], ids[:, 0:first]).then_inc(s_ids, 16)
            sp.dma_start(ids_sb[:, first:], ids[:, first:]).then_inc(s_ids_later, 16)
            sp.dma_start(prow[:], picked_row).then_inc(s_prow, 16)
            for k in range(len(PICKED_ALL)):
                sp.dma_start(tab[k][:], picked_tables[k]).then_inc(s_tab[k], 16)
                if k == 0:
                    sp.dma_start(x_rows[:], x).then_inc(s_x, 16)
            for t in range(1, TURNS):
                if t == 2:
                    sp.wait_ge(s_row[GATHERS - 1], 16)
                sp.dma_start(pid_i[:, t - 1, :], picked_ids[t - 1:t, :].broadcast_to([PICK_P, len(PICKED) * TILE_B]))\
                    .then_inc(s_pid[t], 16)
            sp.dma_start(pid_last[:].rearrange("p k b -> p (k b)"),
                         picked_ids_last.broadcast_to([PICK_P, len(PICKED_ENDS) * TILE_B])).then_inc(s_pid_last, 16)
            sp.dma_start(w1x_sb[:], w1x).then_inc(s_w, 16)
            for g in range(JB):
                sp.wait_ge(s_row[GATHERS + SKIPPED + g], 16)
                sp.dma_start(w1z_sb[:, g, :], w1z[:, g, :]).then_inc(s_w, 16)
            sp.dma_start(w2_sb[:], w2).then_inc(s_w, 16)
            sp.dma_start(w3_sb[:], w3).then_inc(s_w, 16)
            sp.dma_start(b1_sb[:], b1).then_inc(s_w, 16)
            sp.dma_start(b2_sb[:], b2).then_inc(s_w, 16)
            sp.wait_ge(s_y, done(LAST))
            sp.dma_start(out, y_sb[:]).then_inc(s_out, 16)
            sp.wait_ge(s_out, 16)

        @block.gpsimd
        def _(pool):
            nc.gpsimd.memset(ident[:], 0.0).then_inc(s_ident, 1)
            pool.wait_ge(s_ident, 1)
            nc.gpsimd.affine_select(out=ident[:], in_=ident[:], compare_op=ALU.not_equal, fill=1.0, base=0,
                                    pattern=[[-1, P]], channel_multiplier=1).then_inc(s_ident, 1)
            nc.gpsimd.memset(z[:], 0.0).then_inc(s_zero_z, 1)

            def gather(u, gathers):
                for g in gathers:
                    slot = u * GATHERS + g
                    pool.indirect_dma_start(
                        out=rows[:, slot, :], out_offset=None, in_=table,
                        in_offset=bass.IndirectOffsetOnAxis(ap=idx_now[:, u, g:g + 1], axis=0),
                    ).then_inc(s_row[slot], 16)

            for u in range(UNITS):
                pool.wait_ge(s_idx[u], 1)
                gather(u, range(SKIPPED, GATHERS))
            with pool.Fori(1, LAST) as i:
                for u in range(UNITS):
                    pool.wait_ge(s_idx[u], i + 1)
                    pool.sem_inc(s_units, 1)
                    gather(u, range(GATHERS))
            for u in range(UNITS):
                pool.wait_ge(s_idx[u], TURNS)
                gather(u, range(SKIPPED, GATHERS))

        @block.vector
        def _(dve):
            dve.wait_ge(s_ids, 16)
            base = ids_sb[:, 0:GATHERS]
            for u in range(UNITS):
                nc.vector.tensor_tensor(idx_now[:, u, :], ids_sb[:, (1 + u) * GATHERS:(2 + u) * GATHERS], base, ALU.add)\
                    .then_inc(s_idx[u], 1)
            nc.vector.memset(ct[:, :, :, NF:QP], 0.0).then_inc(s_zero, 1)
            for s in [*s_ct[0::2], *s_z_dve, s_y, s_h1_dve, s_h2_dve]:
                dve.sem_inc(s, 1)

            def one_hot_of(ids_now, into):
                return nc.vector.tensor_tensor(
                    into[:], ids_now.broadcast_to([PICK_P, PICK_K, TILE_B]),
                    prow[:].rearrange("p (c a) -> p c a", a=1).broadcast_to([PICK_P, PICK_K, TILE_B]), ALU.is_equal)

            def one_hot(i, tables):
                for k in tables:
                    ids_now = one_turn(pid, i - 1)[:, k * TILE_B:(k + 1) * TILE_B]
                    dve.wait_ge(s_picked[k], i)
                    for c in range(PICK_K):
                        last = nc.vector.tensor_scalar(onehot[k][:, c, :], ids_now, prow[:, c:c + 1], None,
                                                       ALU.is_equal)
                    last.then_inc(s_onehot[k], 1)

            def split(k):
                dve.wait_ge(s_tab[k], 16)
                nc.vector.tensor_tensor(res[k][:], tab[k][:], top_half(tab[k]), ALU.subtract).then_inc(s_res[k], 1)
                dve.wait_ge(s_res[k], 1)
                nc.vector.tensor_tensor(low[k][:], res[k][:], top_half(res[k]), ALU.subtract).then_inc(s_low[k], 1)

            def relu_h1(i):
                dve.wait_ge(s_w, 16 * LOADS)
                dve.wait_ge(s_h2p, done(i - 1))
                dve.wait_ge(s_h1p[0], done(i))
                for n in range(N1 // 2):
                    last = nc.vector.tensor_scalar(h1[:, n, :], p_h1[n], b1_sb[:, n:n + 1], 0.0, ALU.add, ALU.max)
                last.then_inc(s_h1_dve, 1)

            def relu_h2(i):
                dve.wait_ge(s_yp, done(i - 1))
                dve.wait_ge(s_h2p, done(i))
                nc.vector.tensor_scalar(h2[:, 0, :], p_h2[0], b2_sb[:, 0:1], 0.0, ALU.add, ALU.max)\
                    .then_inc(s_h2_dve, 1)

            def copy_y(i):
                dve.wait_ge(s_yp, done(i))
                nc.vector.tensor_copy(y_sb[0:1, samples(i)], p_y).then_inc(s_y, 1)

            def tile(i, u, t):
                copy_tile(dve, nc.vector.tensor_copy, i, u, t)

            def next_indices(i, u):
                for t in range(TPT):
                    dve.wait_ge(s_et[u * TPT + t], done(i - 1))
                nc.vector.tensor_copy(idx_now[:, u, :], idx_all[:, bass.ds((i - 1) * SLOTS + u * GATHERS, GATHERS)])\
                    .then_inc(s_idx[u], 1)

            def products(i, u):
                copy_z(dve, nc.vector.tensor_copy, i, u, range(0, QUADS, 2), s_z_dve)

            dve.wait_ge(s_ids_later, 16)
            later = GATHERS + SLOTS
            nc.vector.tensor_tensor(
                idx_all[:].rearrange("p (v g) -> p v g", g=GATHERS),
                ids_sb[:, later:].rearrange("p (v g) -> p v g", g=GATHERS),
                base.rearrange("p (a g) -> p a g", a=1).broadcast_to([P, (TURNS - 1) * UNITS, GATHERS]),
                ALU.add).then_inc(s_idx_all, 1)
            dve.wait_ge(s_pid[0], 16)
            dve.wait_ge(s_prow, 16)
            for k in range(len(PICKED_ALL)):
                one_hot_of(pid_0[:, k:k + 1, :], onehot_0[k]).then_inc(s_onehot_0[k], 1)
            dve.wait_ge(s_zero, 1)
            dve.wait_ge(s_zero_z, 1)
            split(0)
            split(1)
            dve.wait_ge(s_pid16, 1)
            one_hot(1, [0])
            split(2)
            tile(0, 0, 0)
            tile(0, 0, 2)
            dve.wait_ge(s_idx_all, 1)
            next_indices(1, 0)
            one_hot(1, [1])
            products(0, 0)
            tile(0, 1, 1)
            one_hot(1, [2])
            split(3)
            one_hot(1, [3])
            dve.wait_ge(s_pid16, TURNS - 1)
            with dve.Fori(0, LAST - 1) as i:
                next_indices(i + 1, 1)
                products(i, 1)
                one_hot(i + 2, [0])
                tile(i + 1, 0, 0)
                tile(i + 1, 0, 2)
                next_indices(i + 2, 0)
                one_hot(i + 2, range(1, len(PICKED)))
                relu_h1(i)
                products(i + 1, 0)
                relu_h2(i)
                tile(i + 1, 1, 1)
                copy_y(i)

            def last_one_hot(k):
                split(k)
                n = k - len(PICKED)
                one_hot_of(pid_last[:, n:n + 1, :], onehot[k]).then_inc(s_last_onehot[n], 1)

            next_indices(LAST, 1)
            dve.wait_ge(s_pid_last, 16)
            last_one_hot(len(PICKED))
            products(LAST - 1, 1)
            tile(LAST, 0, 0)
            last_one_hot(len(PICKED) + 1)
            tile(LAST, 0, 2)
            relu_h1(LAST - 1)
            products(LAST, 0)
            tile(LAST, 1, 1)
            relu_h2(LAST - 1)
            copy_last_z(dve, nc.vector.tensor_copy, range(0, QUADS, 2), s_last_z_dve)
            copy_y(LAST - 1)
            for n in range(0, N1, 2):
                dve.wait_ge(s_last_h1p[n], 1)
                nc.vector.tensor_scalar(h1[:, n, :], last_h1[n], b1_sb[:, n:n + 1], 0.0, ALU.add, ALU.max)\
                    .then_inc(s_last_h1[n], 1)
            dve.wait_ge(s_last_h2p[0], 1)
            nc.vector.tensor_scalar(h2[:, 0, :], p_h2[0], b2_sb[:, 0:1], 0.0, ALU.add, ALU.max).then_inc(s_h2_dve, 1)
            copy_y(LAST)

        @block.scalar
        def _(act):
            act.dma_start(pid_0[:].rearrange("p k b -> p (k b)"),
                          picked_ids_0.broadcast_to([PICK_P, len(PICKED_ALL) * TILE_B])).then_inc(s_pid[0], 16)
            for s in [*s_ct[1::2], *s_cx, *s_z_act, s_h1_act, s_h2_act]:
                act.sem_inc(s, 1)

            def narrow_ids(i):
                act.wait_ge(s_pid[i], 16)
                nc.scalar.copy(pid[:, i - 1, :], pid_i[:, i - 1, :]).then_inc(s_pid16, 1)

            def stage(i, h):
                ks = slice(h * HALF, (h + 1) * HALF)
                for k in range(h * HALF, (h + 1) * HALF):
                    act.wait_ge(s_picked[k], i + 1)
                for u in range(UNITS):
                    act.wait_ge(s_cx[u], done(i - 1))
                nc.scalar.copy(picked[:, ks, :], p_pick[:, ks, :]).then_inc(s_stage[h], 1)

            def dense_column(i, u):
                act.wait_ge(s_gram[u], done(i - 1))
                nc.scalar.copy(ct[:, u, :, len(GATHERED)], xt[:, bass.ds(i * TILE_B + u * UNIT_B, UNIT_B)])

            def picked_columns(i, u):
                for h in range(2):
                    act.wait_ge(s_stage[h], i + 1)
                nc.scalar.copy(ct[:, u, :, len(GATHERED) + 1:NF],
                               picked[:, :, u * UNIT_B:(u + 1) * UNIT_B].rearrange("p v s -> p s v"))\
                    .then_inc(s_cx[u], 1)

            def relu_h1(i):
                act.wait_ge(s_w, 16 * LOADS)
                act.wait_ge(s_h2p, done(i - 1))
                act.wait_ge(s_h1p[1], done(i))
                for n in range(N1 // 2, N1):
                    last = nc.scalar.activation(h1[:, n, :], p_h1[n], ACT.Relu, bias=b1_sb[:, n:n + 1])
                last.then_inc(s_h1_act, 1)

            def relu_h2(i):
                act.wait_ge(s_yp, done(i - 1))
                act.wait_ge(s_h2p, done(i))
                nc.scalar.activation(h2[:, 1, :], p_h2[1], ACT.Relu, bias=b2_sb[:, 1:2]).then_inc(s_h2_act, 1)

            def tile(i, u, t):
                copy_tile(act, nc.scalar.copy, i, u, t)

            def products(i, u):
                copy_z(act, nc.scalar.copy, i, u, range(1, QUADS, 2), s_z_act)

            act.wait_ge(s_zero_z, 1)
            act.wait_ge(s_xp, 1)
            nc.scalar.copy(xt[:], p_mlp[2][:].rearrange("p n b -> p (n b)")).then_inc(s_xt, 1)
            narrow_ids(1)
            act.wait_ge(s_zero, 1)
            act.wait_ge(s_xt, 1)
            for h in range(2):
                for u in range(h, UNITS, 2):
                    dense_column(0, u)
                for k in range(h * HALF, (h + 1) * HALF):
                    act.wait_ge(s_picked[k], 1)
                nc.scalar.copy(picked[:, h * HALF:(h + 1) * HALF, :], p_pick_0[h]).then_inc(s_stage[h], 1)
            for u in range(UNITS):
                for k in range(len(PICKED), len(PICKED_ALL)):
                    act.wait_ge(s_picked[k], 1)
                nc.scalar.copy(ct[:, u, :, 0:len(PICKED_ENDS)],
                               p_pick_0[2][:, :, u * UNIT_B:(u + 1) * UNIT_B].rearrange("p v s -> p s v"))
                picked_columns(0, u)
                if u == 0:
                    tile(0, 0, 1)
            products(0, 0)
            tile(0, 1, 0)
            for t in range(2, TURNS):
                narrow_ids(t)
            with act.Fori(0, LAST - 1) as i:
                tile(i, 1, 2)
                stage(i + 1, 0)
                products(i, 1)
                stage(i + 1, 1)
                for u in range(UNITS):
                    dense_column(i + 1, u)
                    picked_columns(i + 1, u)
                tile(i + 1, 0, 1)
                relu_h1(i)
                products(i + 1, 0)
                relu_h2(i)
                tile(i + 1, 1, 0)
            tile(LAST - 1, 1, 2)
            stage(LAST, 0)
            products(LAST - 1, 1)
            stage(LAST, 1)
            for u in range(UNITS):
                dense_column(LAST, u)
                picked_columns(LAST, u)
            relu_h1(LAST - 1)
            act.wait_ge(s_last_picked, len(PICKED_ENDS))
            for u in range(UNITS):
                nc.scalar.copy(ct[:, u, :, 0:len(PICKED_ENDS)],
                               p_pick[:, 0:len(PICKED_ENDS), u * UNIT_B:(u + 1) * UNIT_B].rearrange("p v s -> p s v"))\
                    .then_inc(s_last_columns[u], 1)
            tile(LAST, 0, 1)
            tile(LAST, 1, 0)
            products(LAST, 0)
            tile(LAST, 1, 2)
            relu_h2(LAST - 1)
            copy_last_z(act, nc.scalar.copy, range(1, QUADS, 2), s_last_z_act)
            for n in range(1, N1, 2):
                act.wait_ge(s_last_h1p[n], 1)
                nc.scalar.activation(h1[:, n, :], last_h1[n], ACT.Relu, bias=b1_sb[:, n:n + 1])\
                    .then_inc(s_last_h1[n], 1)
            act.wait_ge(s_last_h2p[1], 1)
            nc.scalar.activation(h2[:, 1, :], p_h2[1], ACT.Relu, bias=b2_sb[:, 1:2]).then_inc(s_h2_act, 1)

        @block.tensor
        def _(pe):
            for s in [*s_et, *s_gram, *s_h1p, s_h2p, s_yp]:
                pe.sem_inc(s, 1)

            def first_pick(k):
                pe.wait_ge(s_tab[k], 16)
                pe.wait_ge(s_onehot_0[k], 1)
                own = k >= len(PICKED)
                bank, place = (2, k - len(PICKED)) if own else divmod(k, HALF)
                for c in range(PICK_K):
                    last = nc.tensor.matmul(p_pick_0[bank][:, place, :], tab[k][:, c, :], onehot_0[k][:, c, :],
                                            start=(c == 0), stop=(c == PICK_K - 1))
                last.then_inc(s_picked[k], 1)

            def pick_parts(k, place):
                for n, part in enumerate((top_half(tab[k]), top_half(res[k]), low[k])):
                    for c in range(PICK_K):
                        last = nc.tensor.matmul(p_pick[:, place, :], part[:, c, :], onehot[k][:, c, :],
                                                start=(n == 0 and c == 0), stop=(n == 2 and c == PICK_K - 1))
                return last

            def pick(i, tables):
                for k in tables:
                    pe.wait_ge(s_stage[1 if k < HALF else 0], i if k < HALF else i + 1)
                    pe.wait_ge(s_res[k], 1)
                    pe.wait_ge(s_low[k], 1)
                    pe.wait_ge(s_onehot[k], i)
                    pick_parts(k, k).then_inc(s_picked[k], 1)

            def keep_warm(into, count):
                for _ in range(count):
                    nc.tensor.transpose(into, ident[:], ident[:])

            def transposes(i, u, tiles, warm=0):
                for t in tiles:
                    tile = u * TPT + t
                    before = (tile - ET_BANKS) % TILES
                    pe.wait_ge(s_ct[before], done(i) if before < tile else done(i - 1))
                    for k, g in enumerate(gathers_of(t)):
                        if k < skipped(i, t):
                            continue
                        slot = u * GATHERS + g
                        keep_warm(p_warm, warm)
                        pe.wait_ge(s_row[slot], 16 * (i if g < SKIPPED else i + 1))
                        last = nc.tensor.transpose(p_et[tile % ET_BANKS][:, k * P:(k + 1) * P], rows[:, slot, :],
                                                   ident[:])
                    last.then_inc(s_et[tile], 1)

            def products(i, u):
                for t in range(TPT):
                    pe.wait_ge(s_ct[u * TPT + t], done(i))
                pe.wait_ge(s_cx[u], done(i))
                pe.wait_ge(s_z_dve[u], done(i - 1))
                pe.wait_ge(s_z_act[u], done(i - 1))
                for b in range(CLASS_B):
                    for s in range(QUADS):
                        v = ct[:, u, s * CLASS_B + b, :]
                        last = nc.tensor.matmul(p_gram[u][QP * s:QP * s + NF, b, :], v[:, 0:NF], v[:, 0:GW],
                                                start=True, stop=True)
                last.then_inc(s_gram[u], 1)

            def layer1(i, half):
                pe.wait_ge(s_w, 16 * LOADS)
                pe.wait_ge((s_h1_dve, s_h1_act)[half], done(i - 1))
                if half == 0:
                    pe.wait_ge(s_h2_act, done(i - 1))
                for n in range(half * N1 // 2, (half + 1) * N1 // 2):
                    nc.tensor.matmul(p_h1[n], w1x_sb[:, n * P:(n + 1) * P], xt[:, samples(i)], start=True, stop=False)
                    if half == 1 and n == N1 // 2:
                        for u in range(UNITS):
                            pe.wait_ge(s_z_dve[u], done(i))
                            pe.wait_ge(s_z_act[u], done(i))
                    for g in range(JB):
                        last = nc.tensor.matmul(p_h1[n], w1z_sb[:, g, n * P:(n + 1) * P], z[:, g, :],
                                                start=False, stop=(g == JB - 1))
                last.then_inc(s_h1p[half], 1)

            def h2_block(n, ks):
                for k in ks:
                    last = nc.tensor.matmul(p_h2[n], w2_sb[:, k, n * P:(n + 1) * P], h1[:, k, :],
                                            start=(k == 0), stop=(k == N1 - 1))
                return last

            def layer2(i):
                pe.wait_ge(s_y, done(i - 1))
                pe.wait_ge(s_h1_dve, done(i))
                pe.wait_ge(s_h1_act, done(i))
                for n in range(N2):
                    last = h2_block(n, range(N1))
                last.then_inc(s_h2p, 1)

            def layer3(i):
                for k in range(N2):
                    pe.wait_ge((s_h2_dve, s_h2_act)[k], done(i))
                    last = nc.tensor.matmul(p_y, w3_sb[:, k:k + 1], h2[:, k, :], start=(k == 0), stop=(k == N2 - 1))
                last.then_inc(s_yp, 1)

            pe.wait_ge(s_ident, 2)
            keep_warm(p_warm, WARM_UP)
            for k in range(HALF):
                first_pick(k)
            pe.wait_ge(s_x, 16)
            for t in range(B // P):
                last = nc.tensor.transpose(p_mlp[2][:, t, :], x_rows[:, t, :], ident[:])
            last.then_inc(s_xp, 1)
            for k in range(HALF, len(PICKED_ALL)):
                first_pick(k)
            transposes(0, 0, range(TPT))
            pe.wait_ge(s_xt, 1)
            pe.wait_ge(s_zero, 1)
            keep_warm(p_warm, WARM_PRODUCTS)
            products(0, 0)
            transposes(0, 1, range(TPT - 1), WARM_ROW)
            with pe.Fori(0, LAST - 1) as i:
                pick(i + 1, [0])
                transposes(i, 1, [TPT - 1])
                pick(i + 1, [1])
                products(i, 1)
                pick(i + 1, range(HALF, len(PICKED)))
                transposes(i + 1, 0, [0])
                layer1(i, 1)
                transposes(i + 1, 0, range(1, TPT))
                layer1(i, 0)
                products(i + 1, 0)
                layer2(i)
                transposes(i + 1, 1, range(TPT - 1))
                layer3(i)

            def dense_h1(n):
                nc.tensor.matmul(last_h1[n], w1x_sb[:, n * P:(n + 1) * P], xt[:, LAST * TILE_B:], start=True, stop=False)

            pick(LAST, [0])
            transposes(LAST - 1, 1, [TPT - 1])
            pick(LAST, [1])
            products(LAST - 1, 1)
            pick(LAST, range(HALF, len(PICKED)))
            transposes(LAST, 0, [0])
            layer1(LAST - 1, 1)
            pe.wait_ge(s_stage[1], TURNS)
            for n in range(len(PICKED_ENDS)):
                k = len(PICKED) + n
                pe.wait_ge(s_res[k], 1)
                pe.wait_ge(s_low[k], 1)
                pe.wait_ge(s_last_onehot[n], 1)
                pick_parts(k, n).then_inc(s_last_picked, 1)
            transposes(LAST, 0, range(1, TPT))
            layer1(LAST - 1, 0)
            transposes(LAST, 1, [0])
            pe.wait_ge(s_last_columns[0], 1)
            products(LAST, 0)
            transposes(LAST, 1, [1])
            pe.wait_ge(s_y, done(LAST - 2))
            pe.wait_ge(s_h1_dve, done(LAST - 1))
            pe.wait_ge(s_h1_act, done(LAST - 1))
            h2_block(0, range(N1))
            transposes(LAST, 1, [TPT - 1])
            h2_block(1, range(N1)).then_inc(s_h2p, 1)
            pe.wait_ge(s_last_columns[1], 1)
            for t in range(TPT):
                pe.wait_ge(s_ct[TPT + t], done(LAST))
            pe.wait_ge(s_cx[1], done(LAST))
            for h in range(2):
                pe.wait_ge(s_z_dve[1 - h], done(LAST - 1 + h))
                pe.wait_ge(s_z_act[1 - h], done(LAST - 1 + h))
                for b in range(CLASS_B // 2):
                    for s in range(QUADS):
                        v = ct[:, 1, s * CLASS_B + h * CLASS_B // 2 + b, :]
                        last = nc.tensor.matmul(p_gram[1 - h][QP * s:QP * s + NF, b, :], v[:, 0:NF], v[:, 0:GW],
                                                start=True, stop=True)
                last.then_inc(s_last_gram[h], 1)
            layer3(LAST - 1)
            for n in range(N1):
                dense_h1(n)
            for s in (s_last_z_dve, s_last_z_act):
                pe.wait_ge(s, 1)
            for n in range(N1):
                for g in range(JB):
                    last = nc.tensor.matmul(last_h1[n], w1z_sb[:, g, n * P:(n + 1) * P], z[:, g, :],
                                            start=False, stop=(g == JB - 1))
                last.then_inc(s_last_h1p[n], 1)
            pe.wait_ge(s_y, done(LAST - 1))
            for n in range(N2):
                for k in range(N1):
                    if n == 0:
                        pe.wait_ge(s_last_h1[k], 1)
                    last = h2_block(n, [k])
                last.then_inc(s_last_h2p[n], 1)
            layer3(LAST)


def kernel(**inputs):
    import concourse.bacc as bacc
    from concourse.bass_utils import run_bass_kernel_spmd

    a = {k: np.asarray(v) for k, v in inputs.items()}
    tables = [a[f"tbl_{f}"] for f in GATHERED]
    starts = np.cumsum([0] + [t.shape[0] for t in tables[:-1]])
    ids = a["ids"][:, GATHERED].reshape(B // UNIT_B, UNIT_B, GATHERS, FPG).transpose(3, 1, 0, 2)
    base = np.repeat(starts.reshape(GATHERS, FPG).T, UNIT_B, axis=0).astype(np.int32)
    low, high = np.triu_indices(NF, k=1)
    pair = np.full((NF, NF), PAIRS)
    pair[low, high] = pair[high, low] = np.arange(PAIRS)
    rows = np.full((QUADS, QP, JB), PAIRS)
    for f in range(NF):
        for g in range(f + 1, NF):
            rows[g // JB, f, g % JB] = pair[VECTORS[f], VECTORS[g]]
    w1 = a["W_top1"]
    padded = np.concatenate([w1[:PAIRS], np.zeros((1, H1), w1.dtype)])
    arrays = {
        "x": a["r_dense_x"].reshape(B // P, P, D).transpose(1, 0, 2),
        "ids": np.concatenate([base, ids.reshape(P, TURNS * SLOTS)], axis=1),
        "picked_ids_0": a["ids"][:TILE_B, PICKED_ALL].T.reshape(1, -1),
        "picked_ids": a["ids"][TILE_B:, PICKED].reshape(LAST, TILE_B, len(PICKED)).transpose(0, 2, 1).reshape(LAST, -1),
        "picked_ids_last": a["ids"][LAST * TILE_B:, PICKED_ENDS].T.reshape(1, -1),
        "picked_row": np.arange(PICKED_ROWS, dtype=np.float32).reshape(PICK_P, PICK_K),
        "picked_tables": np.stack([a[f"tbl_{f}"].reshape(PICK_P, PICK_K, D) for f in PICKED_ALL]),
        "table": np.concatenate(tables),
        "w1z": padded[rows.reshape(P, JB)],
        "w1x": w1[PAIRS:],
        "b1": a["b_top1"].reshape(N1, P).T,
        "w2": a["W_top2"].reshape(N1, P, H2).transpose(1, 0, 2),
        "b2": a["b_top2"].reshape(N2, P).T,
        "w3": a["W_top3"].reshape(N2, P).T,
    }
    arrays = {k: np.ascontiguousarray(v) for k, v in arrays.items()}

    nc = bacc.Bacc("TRN2", target_bir_lowering=False, num_devices=1)
    args = [nc.dram_tensor(k, v.shape, mybir.dt.from_np(v.dtype), kind="ExternalInput").ap() for k, v in arrays.items()]
    out = nc.dram_tensor("y", (1, B), mybir.dt.float32, kind="ExternalOutput").ap()
    interaction_kernel(nc, *args, out)
    r = run_bass_kernel_spmd(nc, [arrays], core_ids=[0])
    return r.results[0]["y"].reshape(B, 1)
```
